# Optimizing a Trainium2 kernel written in Bass

```python
import numpy as np
import jax
import jax.numpy as jnp

def _softmax(x, axis=-1):
    return jax.nn.softmax(x, axis=axis)

def _gelu(x):
    return jax.nn.gelu(x, approximate=True)

def _silu(x):
    return jax.nn.silu(x)

def _sigmoid(x):
    return jax.nn.sigmoid(x)

def _layernorm(x, axis=-1, eps=1e-05):
    m = jnp.mean(x, axis=axis, keepdims=True)
    v = jnp.var(x, axis=axis, keepdims=True)
    return (x - m) / jnp.sqrt(v + eps)

def _scatter_add(tgt, idx, src, axis=0):
    return tgt.at[idx].add(src)

def _segment_sum(src, seg, n):
    return jax.ops.segment_sum(src, seg, n)
kernel_name = 'mk_gnn_ffn_d2_gnn_r32_c51755'

def setup_inputs(seed: int=0):
    np.random.seed(seed)
    _w = jnp.asarray

    def _rec_inputs():
        import jax
        import jax.numpy as jnp
        _gk = jax.random.key(seed)
        x = -0.0002117 + 1 * jax.random.normal(jax.random.fold_in(_gk, 1), (3125, 256), jnp.float32)
        src = jax.random.randint(jax.random.fold_in(_gk, 2), (50000,), 0, 3125, jnp.int32)
        dst = jax.random.randint(jax.random.fold_in(_gk, 3), (50000,), 0, 3125, jnp.int32)
        _o = jnp.argsort(dst, stable=True)
        src = src[_o]
        dst = dst[_o]
        edge_weight = jax.random.uniform(jax.random.fold_in(_gk, 13), (50000,), jnp.float32, 0.0, 0.999998)
        return (x, src, dst, edge_weight)
    x, src, dst, edge_weight = _rec_inputs()

    def _L0_gnn_setup():
        import jax, jax.numpy as jnp
        import numpy as np
        N, D, E = (3125, 256, 312500)
        H = 2 * D
        EPS = 0.0
        key = jax.random.key(seed)
        k1, k2, k3, k4, k5, k6, k7 = jax.random.split(key, 7)
        x = jax.random.normal(k1, (N, D), dtype=jnp.float32)
        edge_index = jax.random.randint(k2, (2, E), 0, N, dtype=jnp.int64)
        edge_weight = jax.random.uniform(k3, (E,), dtype=jnp.float32)
        s1 = 1.0 / np.sqrt(D)
        s2 = 1.0 / np.sqrt(H)
        W1 = jax.random.uniform(k4, (D, H), dtype=jnp.float32, minval=-s1, maxval=s1)
        b1 = jax.random.uniform(k5, (H,), dtype=jnp.float32, minval=-s1, maxval=s1)
        W2 = jax.random.uniform(k6, (H, D), dtype=jnp.float32, minval=-s2, maxval=s2)
        b2 = jax.random.uniform(k7, (D,), dtype=jnp.float32, minval=-s2, maxval=s2)
        return {'x': x, 'edge_index': edge_index, 'edge_weight': edge_weight, 'W1': W1, 'b1': b1, 'W2': W2, 'b2': b2}
    _L0_gnn_all = _L0_gnn_setup()
    _L0_gnn_in = {k: v for k, v in _L0_gnn_all.items() if k in ('W1', 'b1', 'W2', 'b2')}
    del _L0_gnn_all

    def _L0_ffn_setup():
        import math
        import jax, jax.numpy as jnp
        import numpy as np
        CAPACITY_FACTOR = 1.25
        key = jax.random.key(seed)
        ks = jax.random.split(key, 5)
        B, L, D, F, E = (8, 256, 256, 1024, 8)
        h = jax.random.normal(ks[0], (B, L, D), dtype=jnp.float32)
        gate_w = jax.random.normal(ks[1], (D, E), dtype=jnp.float32) * 0.02
        gate_b = jnp.zeros((E,), dtype=jnp.float32)
        w1 = jax.random.normal(ks[2], (E, D, F), dtype=jnp.float32) * (1.0 / math.sqrt(D))
        b1 = jnp.zeros((E, F), dtype=jnp.float32)
        w2 = jax.random.normal(ks[3], (E, F, D), dtype=jnp.float32) * (1.0 / math.sqrt(F))
        b2 = jnp.zeros((E, D), dtype=jnp.float32)
        return {'h': h, 'gate_w': gate_w, 'gate_b': gate_b, 'w1': w1, 'b1': b1, 'w2': w2, 'b2': b2}
    _L0_ffn_all = _L0_ffn_setup()
    _L0_ffn_in = {k: v for k, v in _L0_ffn_all.items() if k in ('gate_w', 'gate_b', 'w1', 'b1', 'w2', 'b2')}
    del _L0_ffn_all

    def _L1_gnn_setup():
        import jax, jax.numpy as jnp
        import numpy as np
        N_NODES = 3125
        N_EDGES = 100000
        DIM_IN = 256
        DIM_OUT = 256
        key = jax.random.key(seed)
        ks = jax.random.split(key, 8)
        feat_in = jax.random.normal(ks[0], (N_NODES, DIM_IN), dtype=jnp.float32)
        edge_row = jax.random.randint(ks[1], (N_EDGES,), 0, N_NODES, dtype=jnp.int32)
        edge_col = jax.random.randint(ks[2], (N_EDGES,), 0, N_NODES, dtype=jnp.int32)
        edge_val = jax.random.uniform(ks[3], (N_EDGES,), dtype=jnp.float32)
        s1 = 1.0 / np.sqrt(DIM_IN)
        s2 = 1.0 / np.sqrt(DIM_OUT)
        W1 = jax.random.normal(ks[4], (DIM_IN, DIM_OUT), dtype=jnp.float32) * s1
        b1 = jnp.zeros((DIM_OUT,), dtype=jnp.float32)
        W2 = jax.random.normal(ks[5], (DIM_OUT, DIM_OUT), dtype=jnp.float32) * s2
        b2 = jnp.zeros((DIM_OUT,), dtype=jnp.float32)
        eps = jnp.zeros((1,), dtype=jnp.float32)
        offset = jnp.zeros((DIM_OUT,), dtype=jnp.float32)
        scale = jnp.ones((DIM_OUT,), dtype=jnp.float32)
        return {'feat_in': feat_in, 'edge_row': edge_row, 'edge_col': edge_col, 'edge_val': edge_val, 'W1': W1, 'b1': b1, 'W2': W2, 'b2': b2, 'eps': eps, 'offset': offset, 'scale': scale}
    _L1_gnn_all = _L1_gnn_setup()
    _L1_gnn_in = {k: v for k, v in _L1_gnn_all.items() if k in ('W1', 'b1', 'W2', 'b2', 'eps', 'offset', 'scale')}
    del _L1_gnn_all

    def _L1_ffn_setup():
        import jax, jax.numpy as jnp
        import numpy as np
        BN_EPS = 0.001

        def _bn(h, g, b, m, v):
            return g * (h - m) * jax.lax.rsqrt(v + BN_EPS) + b
        key = jax.random.key(seed)
        ks = jax.random.split(key, 8)
        B, F, Df = (256, 64, 256)
        E, H, D = (8, 256, 256)
        s1 = 1.0 / np.sqrt(Df)
        s2 = 1.0 / np.sqrt(H)
        return {'x': jax.random.normal(ks[0], (B, F, Df), jnp.float32), 'Wr': jax.random.normal(ks[1], (Df, E), jnp.float32) * s1, 'br': jnp.zeros((E,), jnp.float32), 'W1': jax.random.normal(ks[2], (E, Df, H), jnp.float32) * s1, 'b1': jnp.zeros((E, H), jnp.float32), 'g1': jnp.ones((E, H), jnp.float32), 'be1': jnp.zeros((E, H), jnp.float32), 'm1': jnp.zeros((E, H), jnp.float32), 'v1': jnp.ones((E, H), jnp.float32), 'W2': jax.random.normal(ks[3], (E, H, H), jnp.float32) * s2, 'b2': jnp.zeros((E, H), jnp.float32), 'g2': jnp.ones((E, H), jnp.float32), 'be2': jnp.zeros((E, H), jnp.float32), 'm2': jnp.zeros((E, H), jnp.float32), 'v2': jnp.ones((E, H), jnp.float32), 'Wo': jax.random.normal(ks[4], (E, H, D), jnp.float32) * s2, 'bo': jnp.zeros((E, D), jnp.float32)}
    _L1_ffn_all = _L1_ffn_setup()
    _L1_ffn_in = {k: v for k, v in _L1_ffn_all.items() if k in ('Wr', 'br', 'W1', 'b1', 'g1', 'be1', 'm1', 'v1', 'W2', 'b2', 'g2', 'be2', 'm2', 'v2', 'Wo', 'bo')}
    del _L1_ffn_all
    return {'x': x, 'src': src, 'dst': dst, 'edge_weight': edge_weight, 'L0_gnn_W1': _L0_gnn_in['W1'], 'L0_gnn_b1': _L0_gnn_in['b1'], 'L0_gnn_W2': _L0_gnn_in['W2'], 'L0_gnn_b2': _L0_gnn_in['b2'], 'L0_ffn_gate_w': _L0_ffn_in['gate_w'], 'L0_ffn_gate_b': _L0_ffn_in['gate_b'], 'L0_ffn_w1': _L0_ffn_in['w1'], 'L0_ffn_b1': _L0_ffn_in['b1'], 'L0_ffn_w2': _L0_ffn_in['w2'], 'L0_ffn_b2': _L0_ffn_in['b2'], 'L1_gnn_W1': _L1_gnn_in['W1'], 'L1_gnn_b1': _L1_gnn_in['b1'], 'L1_gnn_W2': _L1_gnn_in['W2'], 'L1_gnn_b2': _L1_gnn_in['b2'], 'L1_gnn_eps': _L1_gnn_in['eps'], 'L1_gnn_offset': _L1_gnn_in['offset'], 'L1_gnn_scale': _L1_gnn_in['scale'], 'L1_ffn_Wr': _L1_ffn_in['Wr'], 'L1_ffn_br': _L1_ffn_in['br'], 'L1_ffn_W1': _L1_ffn_in['W1'], 'L1_ffn_b1': _L1_ffn_in['b1'], 'L1_ffn_g1': _L1_ffn_in['g1'], 'L1_ffn_be1': _L1_ffn_in['be1'], 'L1_ffn_m1': _L1_ffn_in['m1'], 'L1_ffn_v1': _L1_ffn_in['v1'], 'L1_ffn_W2': _L1_ffn_in['W2'], 'L1_ffn_b2': _L1_ffn_in['b2'], 'L1_ffn_g2': _L1_ffn_in['g2'], 'L1_ffn_be2': _L1_ffn_in['be2'], 'L1_ffn_m2': _L1_ffn_in['m2'], 'L1_ffn_v2': _L1_ffn_in['v2'], 'L1_ffn_Wo': _L1_ffn_in['Wo'], 'L1_ffn_bo': _L1_ffn_in['bo']}

def reference(x, src, dst, edge_weight, L0_gnn_W1, L0_gnn_b1, L0_gnn_W2, L0_gnn_b2, L0_ffn_gate_w, L0_ffn_gate_b, L0_ffn_w1, L0_ffn_b1, L0_ffn_w2, L0_ffn_b2, L1_gnn_W1, L1_gnn_b1, L1_gnn_W2, L1_gnn_b2, L1_gnn_eps, L1_gnn_offset, L1_gnn_scale, L1_ffn_Wr, L1_ffn_br, L1_ffn_W1, L1_ffn_b1, L1_ffn_g1, L1_ffn_be1, L1_ffn_m1, L1_ffn_v1, L1_ffn_W2, L1_ffn_b2, L1_ffn_g2, L1_ffn_be2, L1_ffn_m2, L1_ffn_v2, L1_ffn_Wo, L1_ffn_bo):
    import jax
    import jax.numpy as jnp

    def _L0_gnn_ref(x, edge_index, edge_weight, W1, b1, W2, b2):
        import jax, jax.numpy as jnp
        import numpy as np
        N, D, E = (3125, 256, 312500)
        H = 2 * D
        EPS = 0.0
        row, col = (edge_index[0], edge_index[1])
        messages = x[col] * edge_weight[:, None]
        agg = jax.ops.segment_sum(messages, row, num_segments=N)
        h = (1.0 + EPS) * x + agg
        h = jax.nn.relu(h @ W1 + b1)
        out = h @ W2 + b2
        return out

    def _L0_ffn_ref(h, gate_w, gate_b, w1, b1, w2, b2):
        import math
        import jax, jax.numpy as jnp
        import numpy as np
        CAPACITY_FACTOR = 1.25
        B, L, D = h.shape
        E = gate_w.shape[1]
        T = B * L
        C = max(1, math.ceil(CAPACITY_FACTOR * T / E))
        x = h.reshape(T, D)
        logits = x @ gate_w + gate_b
        probs = jax.nn.softmax(logits, axis=-1)
        idx = jnp.argmax(probs, axis=-1)
        prb = jnp.take_along_axis(probs, idx[:, None], axis=1)[:, 0]
        one_hot = jax.nn.one_hot(idx, E, dtype=jnp.float32)
        pos = (jnp.cumsum(one_hot, axis=0) * one_hot).sum(-1).astype(jnp.int32) - 1
        kept = pos < C
        pos_safe = jnp.where(kept, pos, C)
        buf = jnp.zeros((E, C, D), dtype=h.dtype).at[idx, pos_safe].set(x, mode='drop')
        hmid = jax.nn.relu(jnp.einsum('ecd,edf->ecf', buf, w1) + b1[:, None, :])
        ybuf = jnp.einsum('ecf,efd->ecd', hmid, w2) + b2[:, None, :]
        pos_g = jnp.minimum(pos, C - 1)
        y_tok = ybuf[idx, pos_g] * (prb * kept)[:, None]
        y = y_tok.reshape(B, L, D)
        y = jnp.nan_to_num(y, nan=0.0, posinf=10000.0, neginf=-10000.0)
        return y

    def _L1_gnn_ref(feat_in, edge_row, edge_col, edge_val, W1, b1, W2, b2, eps, offset, scale):
        import jax, jax.numpy as jnp
        import numpy as np
        N_NODES = 3125
        N_EDGES = 100000
        DIM_IN = 256
        DIM_OUT = 256
        msg = edge_val[:, None] * feat_in[edge_col]
        aggr = jax.ops.segment_sum(msg, edge_row, num_segments=feat_in.shape[0])
        aggr = aggr + (1.0 + eps) * feat_in
        h = jnp.maximum(aggr @ W1 + b1, 0.0) @ W2 + b2
        h = jnp.maximum(h, 0.0)
        mean = jnp.mean(h, axis=1, keepdims=True)
        var = jnp.var(h, axis=1, keepdims=True) + 1e-10
        return (h - mean) * scale * jax.lax.rsqrt(var) + offset

    def _L1_ffn_ref(x, Wr, br, W1, b1, g1, be1, m1, v1, W2, b2, g2, be2, m2, v2, Wo, bo):
        import jax, jax.numpy as jnp
        import numpy as np
        BN_EPS = 0.001

        def _bn(h, g, b, m, v):
            return g * (h - m) * jax.lax.rsqrt(v + BN_EPS) + b
        feat = jnp.mean(x, axis=0)
        w = jax.nn.softmax(feat @ Wr + br, axis=-1)
        h = jnp.einsum('bfd,edh->bfeh', x, W1) + b1
        h = jax.nn.relu(_bn(h, g1, be1, m1, v1))
        h = jnp.einsum('bfeh,ehk->bfek', h, W2) + b2
        h = jax.nn.relu(_bn(h, g2, be2, m2, v2))
        y = jnp.einsum('bfeh,ehd->bfed', h, Wo) + bo
        return jnp.einsum('bfed,fe->bfd', y, w)
    edge_index = jnp.stack([src, dst])
    x = x + _L0_gnn_ref(_layernorm(x, axis=-1), edge_index, edge_weight, L0_gnn_W1, L0_gnn_b1, L0_gnn_W2, L0_gnn_b2)
    x = x + _L0_ffn_ref(_layernorm(x, axis=-1)[None], L0_ffn_gate_w, L0_ffn_gate_b, L0_ffn_w1, L0_ffn_b1, L0_ffn_w2, L0_ffn_b2)[0]
    x = x + _L1_gnn_ref(_layernorm(x, axis=-1), src, dst, edge_weight, L1_gnn_W1, L1_gnn_b1, L1_gnn_W2, L1_gnn_b2, L1_gnn_eps, L1_gnn_offset, L1_gnn_scale)
    x = x + _L1_ffn_ref(_layernorm(x, axis=-1)[None], L1_ffn_Wr, L1_ffn_br, L1_ffn_W1, L1_ffn_b1, L1_ffn_g1, L1_ffn_be1, L1_ffn_m1, L1_ffn_v1, L1_ffn_W2, L1_ffn_b2, L1_ffn_g2, L1_ffn_be2, L1_ffn_m2, L1_ffn_v2, L1_ffn_Wo, L1_ffn_bo)[0]
    return x

_drawn_inputs = setup_inputs


def setup_inputs(seed=0):
    import zlib

    import numpy as np

    out = dict(_drawn_inputs(seed))
    spreads = {'L0_ffn_gate_b': (0.0, 0.1),
     'L0_ffn_b1': (0.0, 0.685),
     'L0_ffn_b2': (0.0, 0.453),
     'L1_gnn_b1': (0.0, 0.411),
     'L1_gnn_b2': (0.0, 0.1),
     'L1_gnn_offset': (0.0, 0.1),
     'L1_gnn_scale': (1.0, 0.2),
     'L1_ffn_br': (0.0, 0.8),
     'L1_ffn_b1': (0.0, 0.548),
     'L1_ffn_g1': (1.0, 0.556),
     'L1_ffn_be1': (0.0, 0.593),
     'L1_ffn_m1': (0.0, 0.552),
     'L1_ffn_v1': (1.0, 0.6),
     'L1_ffn_b2': (0.0, 0.4),
     'L1_ffn_g2': (1.0, 0.55),
     'L1_ffn_be2': (0.0, 0.449),
     'L1_ffn_m2': (0.0, 0.4),
     'L1_ffn_v2': (1.0, 0.6),
     'L1_ffn_bo': (0.0, 0.301)}
    factors = {}
    for name, (base, spread) in spreads.items():
        noise = np.random.default_rng([zlib.crc32(name.encode()), seed]).standard_normal(out[name].shape)
        drawn = base * np.exp(spread * noise) if base else spread * noise
        out[name] = jnp.asarray(drawn.astype(out[name].dtype))
    for name, factor in factors.items():
        out[name] = (out[name] * factor).astype(out[name].dtype)
    return out
```

```python
from contextlib import ExitStack

import concourse.bass as bass
from concourse import mybir

F32 = mybir.dt.float32
I32 = mybir.dt.int32
U32 = mybir.dt.uint32
ALU = mybir.AluOpType
ACT = mybir.ActivationFunctionType
AX = mybir.AxisListType
ds = bass.ds

N, D, E = 3125, 256, 50000
P = 128
KD = D // P
TP = 125
NT = N // TP
GT = 5
NG = NT // GT
GN = GT * TP
PIECES = ((0, 375), (375, 250))
EP = 125
EC = E // EP
STAGE = 8
CH = 128
NCH = -(-(E // CH + 1 + NT) // (2 * STAGE)) * 2 * STAGE
RING = 16
BANKS = 8
H0 = 512
H1 = 256
NE = 8
F0 = 1024
CAP = -(-5 * N // (4 * NE))
SLOTS = 512
TRASH = NE * SLOTS
MAGIC = 12582912.0
COLS = {}
for _name, _n in (("g0b1", H0 // P), ("f0b1", NE * F0 // P), ("g1b1", H1 // P),
                  *((f"{v}{l}", NE * KD) for l in (1, 2) for v in ("g", "be", "m", "v", "b"))):
    COLS[_name] = (sum(n for _, n in COLS.values()), _n)
NCOL = sum(n for _, n in COLS.values())
ROWS = {}
for _name, _n in (("g0b2", D), ("g1b2", D), ("offset", D), ("scale", D), ("gate_b", NE), ("br", NE), ("eps", 1)):
    ROWS[_name] = (sum(n for _, n in ROWS.values()), _n)
NROW = sum(n for _, n in ROWS.values())


class Chain:

    def __init__(self, eng, sem):
        self.eng, self.sem, self.n, self.loop = eng, sem, 0, None

    def enter(self, i, per):
        self.loop, self.k = (i, per), 0

    def leave(self, count):
        per = self.loop[1]
        assert self.k == per, (self.k, per)
        self.loop, self.n = None, self.n + count * per

    def link(self, ins):
        ins.then_inc(self.sem, 1)
        if self.loop is None:
            self.n += 1
            self.eng.wait_ge(self.sem, self.n)
        else:
            self.k += 1
            self.eng.wait_ge(self.sem, self.loop[0] * self.loop[1] + (self.n + self.k))


def program(nc, a, out):
    with ExitStack() as ctx:
        def sb(name, shape, dt=F32):
            return ctx.enter_context(nc.sbuf_tensor(name, shape, dt))

        def sem(name):
            return ctx.enter_context(nc.semaphore(name))

        def dram(name, shape, dt=F32):
            return nc.dram_tensor(name, shape, dt, kind="Internal").ap()

        xn_dram = dram("xn_dram", [N, D])
        rec_dram = dram("rec_dram", [CH * NCH, 4])
        rec_rows = rec_dram.rearrange("(p c) w -> p (c w)", p=CH)
        tok_dram = dram("tok_dram", [TRASH + N, D])
        y_dram = dram("y_dram", [NE * CAP, D])

        X = sb("X", [TP, NT, D])
        AGG = sb("AGG", [TP, NT, D])
        WB = sb("WB", [P, 3 * NE * KD * D])
        fw1 = [WB[:, b * 4096:b * 4096 + 2048].rearrange("p (k f) -> p k f", k=KD) for b in range(2)]
        fw2 = [WB[:, b * 4096 + 2048:b * 4096 + 4096].rearrange("p (k f) -> p k f", k=F0 // P) for b in range(2)]
        WE = WB[:].rearrange("p (l e k f) -> p l e k f", l=3, e=NE, k=KD)
        YG = WB[0:TP, 0:NT * D].rearrange("p (t d) -> p t d", t=NT)
        HB = sb("HB", [P, F0 // P * CAP])
        XNT = sb("XNT", [P, KD, N])
        hid = [HB[:].rearrange("p (m c) -> p m c", m=F0 // P),
               XNT[:].rearrange("p k n -> p (k n)")[:, 0:F0 // P * CAP].rearrange("p (m c) -> p m c", m=F0 // P)]
        gh = HB[:, 0:4 * GN].rearrange("p (m n) -> p m n", m=4)
        eh = [HB[:, b * KD * GN:(b + 1) * KD * GN].rearrange("p (m n) -> p m n", m=KD) for b in range(2)]
        RB = sb("RB", [P, RING * D + 2304])
        gath = RB[:, 0:RING * D].rearrange("p (r d) -> p r d", r=RING)
        xe = [RB[:, b * 1024:(b + 1) * 1024].rearrange("p (j d) -> p j d", j=4) for b in range(2)]
        xet = RB[:, 2048:3072].rearrange("p (k s) -> p k s", k=KD)
        yo = [RB[:, 3072 + b * 1024:3072 + (b + 1) * 1024].rearrange("p (j d) -> p j d", j=4) for b in range(2)]
        fb2 = [RB[:, 5120 + b * D:5120 + (b + 1) * D] for b in range(2)]
        ts5 = RB[0:TP, 0:GT * D].rearrange("p (t d) -> p t d", t=GT)
        xn5 = RB[0:TP, 1280:1280 + GT * D].rearrange("p (t d) -> p t d", t=GT)
        hT = RB[:, 2560:2560 + KD * GN].rearrange("p (k n) -> p k n", k=KD)
        xT5 = RB[:, 3810:3810 + KD * GN].rearrange("p (k n) -> p k n", k=KD)
        bo_b = RB[0:TP, 2560:2560 + NE * D].rearrange("p (e d) -> p e d", e=NE)
        h2buf = [RB[:, 1280 * 0:1250].rearrange("p (m n) -> p m n", m=KD),
                 RB[:, 1280:1280 + 1250].rearrange("p (m n) -> p m n", m=KD)]
        rowsb = sb("rowsb", [P, NROW])
        cols = sb("cols", [P, NCOL])
        gw1 = sb("gw1", [P, KD, H0])
        gw2 = sb("gw2", [P, H0 // P, D])
        gate_w = sb("gate_w", [P, KD, NE])
        wr = sb("wr", [P, KD, NE])
        def edge(k, dt=F32):
            v = HB[0:EP, k * EC:(k + 1) * EC]
            return v if dt == F32 else v.bitcast(dt)
        srcf, tile_of, mask, rank, loc = (edge(k) for k in range(5))
        pos, esrc, edst = (edge(k, I32) for k in (5, 6, 7))
        ew = edge(8)
        recs = XNT[0:EP].rearrange("p k n -> p (k n)")[:, 0:4 * EC].rearrange("p (c w) -> p c w", w=4)
        zeros = XNT[:].rearrange("p k n -> p (k n)")[:, 4 * EC:4 * EC + 2048]
        cnt = sb("cnt", [EP, NT])
        nch = sb("nch", [EP, NT])
        cend = sb("cend", [EP, NT])
        cbase = sb("cbase", [EP, NT])
        zero_nt = sb("zero_nt", [EP, NT])
        chunk_tile = sb("chunk_tile", [1, NCH])
        chunk_tile_i = sb("chunk_tile_i", [1, NCH], I32)
        ciota = sb("ciota", [1, NCH])
        gidx = sb("gidx", [CH, 2, STAGE], I32)
        sidx = sb("sidx", [EP, 2, STAGE], I32)
        srec = sb("srec", [EP, 2, STAGE, 4])
        trec = sb("trec", [CH, NCH + STAGE, 4])
        pick = sb("pick", [CH, RING, TP])
        st5 = sb("st5", [TP, GT, 6])
        mv5 = sb("mv5", [TP, GT, 2])
        var5 = sb("var5", [TP, GT])
        std5 = sb("std5", [TP, GT])
        rstd5 = sb("rstd5", [TP, GT])
        LG = sb("LG", [TP, NT, NE])
        oh = sb("oh", [TP, NT, NE])
        ex = sb("ex", [TP, NT, NE])
        px = sb("px", [TP, NT, NE])
        ctot = sb("ctot", [TP, NT, NE])
        mx = sb("mx", [TP, NT])
        rt = sb("rt", [TP, 8, NT])
        rti = sb("rti", [TP, 2, NT], I32)
        GW = sb("GW", [TP, NT, NE])
        rev = sb("rev", [TP, NE])
        trash = sb("trash", [TP, NT])
        big = RB[0:TP, 5120:5120 + GT * D]
        clamped = RB[0:TP, 0:GT * D]
        fin = RB[0:TP, 1280:1280 + GT * D].bitcast(U32)
        ones = sb("ones", [P, P])
        tri = sb("tri", [P, P])
        ident = sb("ident", [P, P])
        iota_row = sb("iota_row", [P, TP])
        bn = sb("bn", [P, 4, NE * KD])
        bnt = sb("bnt", [P, NE * KD])
        PS = [ctx.enter_context(nc.psum_tensor(f"PS{i}", [128, 512], F32)) for i in range(BANKS)]

        def row(name, parts=TP):
            o, n = ROWS[name]
            return rowsb[0:parts, o:o + n]

        def col(name):
            o, n = COLS[name]
            return cols[:, o:o + n]

        def bcast(v, k, n):
            return v.unsqueeze(1).to_broadcast([v.shape[0], k, n])

        def bcast_in(v, n):
            return v.unsqueeze(2).to_broadcast([v.shape[0], v.shape[1], n])

        s_x = sem("x_loaded")
        s_e = sem("edges_loaded")
        s_w = sem("small_weights_loaded")
        s_w1 = sem("second_graph_weights_loaded")
        s_const = sem("constants_ready")
        s_zero = sem("zeros_ready")
        s_recz = sem("records_zeroed")
        s_tokz = sem("slots_zeroed")
        s_dve = sem("dve_chain")
        s_pchain = sem("pool_chain")
        s_step = {e: sem(f"passed_{e}") for e in ("pool", "act", "dve", "sp")}
        s_cnt = sem("counts_ready")
        s_pre = sem("prefix_ready")
        s_pos = sem("positions_ready")
        s_sidx = sem("scatter_indices_staged")
        s_scat = [sem(f"records_scattered{h}") for h in range(2)]
        s_rec = sem("records_loaded")
        s_bn = sem("bn_sqrt")
        L = ("l0", "l1")
        s_xn = {l: sem(f"{l}_xn_ready") for l in L}
        s_xns = {l: sem(f"{l}_xn_stored") for l in L}
        s_gidx = {l: sem(f"{l}_gather_indices_staged") for l in L}
        s_pick = {l: sem(f"{l}_pick_ready") for l in L}
        s_g = {l: [sem(f"{l}_gathered{i}") for i in range(RING)] for l in L}
        s_mm = {l: sem(f"{l}_chunk_multiplied") for l in L}
        s_acc = {l: sem(f"{l}_chunk_added") for l in L}
        s_ts = {l: sem(f"{l}_tiles_staged") for l in L}
        s_tp = {l: sem(f"{l}_transposed") for l in L}
        s_tev = {l: sem(f"{l}_transpose_copied") for l in L}
        s_p1 = {l: sem(f"{l}_hidden_multiplied") for l in L}
        s_e1 = {l: sem(f"{l}_hidden_copied") for l in L}
        s_p2 = {l: sem(f"{l}_output_multiplied") for l in L}
        s_e2 = {l: sem(f"{l}_output_copied") for l in L}
        s_xn5 = {l: sem(f"{l}_next_xn_ready") for l in L}
        s_plg = {l: sem(f"{l}_logits_multiplied") for l in L}
        s_elg = {l: sem(f"{l}_logits_copied") for l in L}
        s_var = sem("variance_ready")
        s_std = sem("std_ready")
        s_oh = sem("one_hot_ready")
        s_ppos = sem("token_prefix_ready")
        s_ex0 = sem("routing_exp_in")
        s_ex1 = sem("routing_exp_done")
        s_route = sem("routing_ready")
        s_tok = sem("tokens_scattered")
        s_fw = [sem(f"expert_weights_loaded{b}") for b in range(2)]
        s_fx = [sem(f"expert_tokens_loaded{b}") for b in range(2)]
        s_ftp = sem("expert_transposed")
        s_fte = sem("expert_transpose_copied")
        s_fp1 = sem("expert_hidden_multiplied")
        s_fe1 = sem("expert_hidden_copied")
        s_fp2 = sem("expert_output_multiplied")
        s_fe2 = sem("expert_output_copied")
        s_fdone = sem("expert_multiplied")
        s_ys = [sem(f"expert_output_stored{b}") for b in range(2)]
        s_yg = [sem(f"outputs_gathered{g}") for g in range(NG)]
        s_ygused = sem("outputs_used")
        s_ew = sem("dense_expert_weights_loaded")
        s_pa = sem("dense_hidden_multiplied")
        s_ea = sem("dense_hidden_copied")
        s_pc = sem("dense_output_multiplied")
        s_ec = sem("dense_output_copied")
        s_bo = sem("dense_output_biases_loaded")
        s_out = sem("out_stored")
        s_res = sem("result_ready")
        block = ctx.enter_context(nc.Block())

        def alone(eng, name, s, value):
            eng.wait_ge(s, value)
            eng.sem_inc(s_step[name], 1)

        @block.sync
        def _(sp):
            sp.dma_start(esrc, a["src"].rearrange("(p c) -> p c", c=EC)).then_inc(s_e, 16)
            sp.dma_start(edst, a["dst"].rearrange("(p c) -> p c", c=EC)).then_inc(s_e, 16)
            sp.dma_start(ew, a["edge_weight"].rearrange("(p c) -> p c", c=EC)).then_inc(s_e, 16)
            sp.dma_start(X[:], a["x"].rearrange("(t p) d -> p t d", p=TP)).then_inc(s_x, 16)
            sp.dma_start(rowsb[:], a["rows"].partition_broadcast(P)).then_inc(s_w, 16)
            sp.dma_start(cols[:], a["cols"]).then_inc(s_w, 16)
            sp.dma_start(gw1[:], a["L0_gnn_W1"].rearrange("(k p) f -> p k f", p=P)).then_inc(s_w, 16)
            sp.dma_start(gw2[:], a["L0_gnn_W2"].rearrange("(k p) f -> p k f", p=P)).then_inc(s_w, 16)
            sp.dma_start(gate_w[:], a["L0_ffn_gate_w"].rearrange("(k p) f -> p k f", p=P)).then_inc(s_w, 16)
            sp.dma_start(wr[:], a["L1_ffn_Wr"].rearrange("(k p) f -> p k f", p=P)).then_inc(s_w, 16)
            sp.wait_ge(s_zero, 1)
            sp.dma_start(rec_rows, zeros[:, 0:4 * NCH]).then_inc(s_recz, 16)
            for e in range(4):
                sp.dma_start(tok_dram[2 * e * SLOTS:(2 * e + 2) * SLOTS, :].rearrange("(p r) d -> p (r d)", p=P),
                             zeros).then_inc(s_tokz, 16)

            def load_expert(e, b):
                sp.dma_start(fw1[b], a["L0_ffn_w1"][ds(e, 1), :, :].rearrange("e (k p) f -> p (e k) f", p=P)).then_inc(s_fw[b], 16)
                sp.dma_start(fw2[b], a["L0_ffn_w2"][ds(e, 1), :, :].rearrange("e (k p) f -> p (e k) f", p=P)).then_inc(s_fw[b], 16)

            def load_tokens(e, b):
                sp.dma_start(xe[b], tok_dram[ds(e * SLOTS, SLOTS), :].rearrange("(j p) d -> p j d", p=P)).then_inc(s_fx[b], 16)
                sp.dma_start(fb2[b], a["L0_ffn_b2"][ds(e, 1), :].rearrange("e d -> (e d)").partition_broadcast(P)).then_inc(s_fx[b], 16)

            for b in range(2):
                load_expert(b, b)
            sp.wait_ge(s_xn["l0"], 1)
            sp.dma_start(xn_dram.rearrange("(t p) d -> p t d", p=TP), AGG[:]).then_inc(s_xns["l0"], 16)
            for h in range(2):
                sp.wait_ge(s_scat[h], 16 * EC // 2)
            sp.dma_start(trec[:, 0:NCH, :].rearrange("p c w -> p (c w)"), rec_rows).then_inc(s_rec, 16)
            sp.wait_ge(s_p2["l0"], NT)
            sp.dma_start(gw1[:, :, 0:H1], a["L1_gnn_W1"].rearrange("(k p) f -> p k f", p=P)).then_inc(s_w1, 16)
            sp.dma_start(gw2[:, 0:KD, :], a["L1_gnn_W2"].rearrange("(k p) f -> p k f", p=P)).then_inc(s_w1, 16)
            sp.wait_ge(s_tok, 16 * NT)
            for b in range(2):
                load_tokens(b, b)
            with sp.Fori(1, NE // 2) as i:
                for b in range(2):
                    e = i * 2 + b
                    sp.wait_ge(s_fdone, e - 1)
                    sp.wait_ge(s_fe2, (e - 1) * 4 + 2)
                    load_tokens(e, b)
                    load_expert(e, b)
            sp.wait_ge(s_ygused, NG)
            for l, name in enumerate(("L1_ffn_W1", "L1_ffn_W2", "L1_ffn_Wo")):
                for e in range(NE):
                    sp.dma_start(WE[:, l, e], a[name][e].rearrange("(k p) f -> p k f", p=P)).then_inc(s_ew, 16)
            sp.wait_ge(s_xn["l1"], 1)
            sp.dma_start(xn_dram.rearrange("(t p) d -> p t d", p=TP), AGG[:]).then_inc(s_xns["l1"], 16)
            sp.wait_ge(s_ex0, 2)
            sp.dma_start(bo_b, a["L1_ffn_bo"].rearrange("e d -> (e d)").partition_broadcast(TP)).then_inc(s_bo, 16)
            with sp.Fori(0, NG) as g:
                sp.wait_ge(s_res, g + 1)
                sp.dma_start(out[ds(g * GN, GN), :].rearrange("(t p) d -> p t d", p=TP),
                             X[:, ds(g * GT, GT), :]).then_inc(s_out, 16)
            sp.wait_ge(s_out, 16 * NG)

        @block.gpsimd
        def _(pool):
            p = nc.gpsimd
            ch = Chain(pool, s_pchain)
            ch.link(p.memset(ones[:], 1.0))
            p.affine_select(out=tri[:], in_=ones[:], compare_op=ALU.is_gt, fill=0.0, base=0,
                            pattern=[[1, P]], channel_multiplier=-1)
            p.affine_select(out=ident[:], in_=ones[:], compare_op=ALU.is_equal, fill=0.0, base=0,
                            pattern=[[1, P]], channel_multiplier=-1)
            for t, pattern, base, cm in ((iota_row[:], [[1, TP]], 0, 0), (ciota[:], [[1, NCH]], 0, 0),
                                         (rev[:], [[-1, NE]], NE, 0), (trash[:], [[TP, NT]], TRASH, 1)):
                ins = p.iota(t, pattern=pattern, base=base, channel_multiplier=cm, allow_small_or_imprecise_dtypes=True)
            ch.link(ins)
            pool.sem_inc(s_const, 1)
            pool.wait_ge(s_pos, 1)
            pool.wait_ge(s_recz, 16)
            with pool.Fori(0, EC // (2 * STAGE)) as i:
                for h in range(2):
                    alone(pool, "pool", s_sidx, 2 * i + (h + 1))
                    for u in range(STAGE):
                        p.indirect_dma_start(rec_dram, bass.IndirectOffsetOnAxis(ap=sidx[:, h, u:u + 1], axis=0),
                                             srec[:, h, u, :], None).then_inc(s_scat[h], 16)

            def gather_edges(l):
                pool.wait_ge(s_xns[l], 16)
                with pool.Fori(0, NCH // (2 * STAGE)) as i:
                    for h in range(2):
                        alone(pool, "pool", s_gidx[l], 2 * i + (h + 1))
                        for u in range(STAGE):
                            r = h * STAGE + u
                            p.indirect_dma_start(gath[:, r, :], None, xn_dram,
                                                 bass.IndirectOffsetOnAxis(ap=gidx[:, h, u:u + 1], axis=0)).then_inc(s_g[l][r], 16)

            gather_edges("l0")
            pool.wait_ge(s_route, 1)
            pool.wait_ge(s_tokz, 64)
            for t in range(NT):
                p.indirect_dma_start(tok_dram, bass.IndirectOffsetOnAxis(ap=rti[:, 0, t:t + 1], axis=0),
                                     AGG[:, t, :], None).then_inc(s_tok, 16)
            with pool.Fori(0, NE // 2) as i:
                for b in range(2):
                    e = i * 2 + b
                    alone(pool, "pool", s_fe2, e * 4 + 6)
                    pool.dma_start(y_dram[ds(e * CAP, 3 * P), :].rearrange("(j p) d -> p j d", p=P),
                                   yo[b][:, 0:3, :]).then_inc(s_ys[b], 16)
                    pool.dma_start(y_dram[ds(e * CAP + 3 * P, CAP - 3 * P), :],
                                   yo[b][0:CAP - 3 * P, 3, :]).then_inc(s_ys[b], 16)
            for b in range(2):
                pool.wait_ge(s_ys[b], 32 * NE // 2)
            for t in range(NT):
                p.indirect_dma_start(YG[:, t, :], None, y_dram,
                                     bass.IndirectOffsetOnAxis(ap=rti[:, 1, t:t + 1], axis=0)).then_inc(s_yg[t // GT], 16)
            gather_edges("l1")

        @block.scalar
        def _(act):
            s = nc.scalar

            def std(loop):
                act.wait_ge(s_var, loop)
                s.activation(std5[:], var5[:], ACT.Sqrt).then_inc(s_std, 1)

            def stage_scatter(i, h):
                s.copy(srec[:, h, :, :], recs[:, ds((2 * i + h) * STAGE, STAGE), :])
                s.copy(sidx[:, h, :], pos[:, ds((2 * i + h) * STAGE, STAGE)]).then_inc(s_sidx, 1)

            act.wait_ge(s_pos, 1)
            for h in range(2):
                stage_scatter(0, h)
            act.wait_ge(s_bn, 1)
            s.activation(bn[:, 0, :], bn[:, 0, :], ACT.Sqrt)
            s.activation(bn[:, 2, :], bn[:, 2, :], ACT.Sqrt).then_inc(s_bn, 1)
            for first, last, norms in ((1, NG + 1, True), (NG + 1, EC // (2 * STAGE), False)):
                with act.Fori(first, last) as i:
                    for h in range(2):
                        alone(act, "act", s_scat[h], i * (16 * STAGE))
                        stage_scatter(i, h)
                    if norms:
                        std(i)

            def stage_gather(l):
                def stage(i, h):
                    s.copy(gidx[:, h, :], trec[:, ds((2 * i + h) * STAGE, STAGE), 1]).then_inc(s_gidx[l], 1)
                for h in range(2):
                    stage(0, h)
                with act.Fori(1, NCH // (2 * STAGE)) as i:
                    for h in range(2):
                        alone(act, "act", s_mm[l], (2 * i + (h - 1)) * STAGE)
                        stage(i, h)

            def graph_mlp(l, hidden, bias, vars_before):
                np1 = hidden // P * 2
                with act.Fori(0, NG) as g:
                    for t in range(GT):
                        act.wait_ge(s_tp[l], g * (2 * GT) + (t + 1))
                        s.copy(hT[:, :, t * TP:(t + 1) * TP],
                               PS[t % 2][:, 0:2 * TP].rearrange("p (k n) -> p k n", k=KD)).then_inc(s_tev[l], 1)
                    for q in range(np1):
                        m, (o, w) = q // 2, PIECES[q % 2]
                        act.wait_ge(s_p1[l], g * np1 + (q + 1))
                        s.activation(gh[:, m, o:o + w], PS[2 + q % 4][:, 0:w], ACT.Relu,
                                     bias=bias[:, m:m + 1]).then_inc(s_e1[l], 1)
                    k = 1 if l == "l0" else 2
                    for j in range(k):
                        std(g * k + (vars_before + j + 1))
                    for t in range(GT):
                        act.wait_ge(s_tp[l], g * (2 * GT) + (GT + t + 1))
                        s.copy(xT5[:, :, t * TP:(t + 1) * TP],
                               PS[t % 2][:, 0:2 * TP].rearrange("p (k n) -> p k n", k=KD)).then_inc(s_tev[l], 1)

            act.wait_ge(s_rec, 16)
            stage_gather("l0")
            graph_mlp("l0", H0, col("g0b1"), NG)
            act.wait_ge(s_ex0, 1)
            s.activation(ex[:], ex[:], ACT.Exp).then_inc(s_ex1, 1)

            f0b1 = col("f0b1").rearrange("p (e m) -> p e m", e=NE)
            with act.Fori(0, NE // 2) as i:
                for b in range(2):
                    e = i * 2 + b
                    for j in range(4):
                        act.wait_ge(s_ftp, e * 4 + (j + 1))
                        s.copy(xet[:, :, j * P:(j + 1) * P],
                               PS[j % 2][:, 0:2 * P].rearrange("p (k n) -> p k n", k=KD)).then_inc(s_fte, 1)
                    for m in range(F0 // P):
                        alone(act, "act", s_fp1, e * 8 + (m + 1))
                        s.activation(hid[b][:, m, :], PS[2 + m % 4][:, 0:CAP], ACT.Relu,
                                     bias=f0b1[:, ds(e, 1), m]).then_inc(s_fe1, 1)
            with act.Fori(0, NG) as g:
                std(g + (2 * NG + 1))
            stage_gather("l1")
            graph_mlp("l1", H1, col("g1b1"), 3 * NG)
            act.wait_ge(s_ex0, 2)
            s.activation(ex[:], ex[:], ACT.Exp).then_inc(s_ex1, 1)

            def relu_norm(j, layer, e, q0):
                for q in range(4):
                    m, (o, w) = q // 2, PIECES[q % 2]
                    act.wait_ge(s_pa, j + (q0 + q + 1))
                    dst = (eh if layer == 0 else h2buf)[e % 2]
                    s.activation(dst[:, m, o:o + w], PS[q][:, 0:w], ACT.Relu,
                                 bias=bn[:, 2 * layer + 1, e * KD + m:e * KD + m + 1],
                                 scale=bn[:, 2 * layer, e * KD + m:e * KD + m + 1]).then_inc(s_ea, 1)
            with act.Fori(0, NG) as g:
                for e in range(NE):
                    relu_norm(g * (8 * NE), 0, e, 8 * e)
                    relu_norm(g * (8 * NE), 1, e, 8 * e + 4)

        @block.tensor
        def _(pe):
            t_ = nc.tensor
            pe.wait_ge(s_cnt, 1)
            pe.wait_ge(s_const, 1)
            t_.matmul(PS[0][0:EP, 0:NT], tri[0:EP, 0:EP], cnt[:], start=True, stop=True)
            t_.matmul(PS[1][0:EP, 0:NT], ones[0:EP, 0:EP], cnt[:], start=True, stop=True).then_inc(s_pre, 1)

            def sum_edges(l):
                with pe.Fori(0, NCH // RING) as i:
                    for u in range(RING):
                        c = i * RING + u
                        pe.wait_ge(s_pick[l], c + 1)
                        pe.wait_ge(s_g[l][u], i * 16 + 16)
                        pe.wait_ge(s_acc[l], c + 1)
                        t_.matmul(PS[u % BANKS][0:TP, 0:D], pick[:, u, :], gath[:, u, :],
                                  start=True, stop=True).then_inc(s_mm[l], 1)

            def turn(l, src, t, n, first):
                bank = PS[t % 2]
                pe.wait_ge(s_tev[l], n + 1)
                for k in range(KD):
                    ins = t_.transpose(bank[:, k * TP:(k + 1) * TP], src[:, t, k * P:(k + 1) * P], ident[0:TP, 0:TP])
                ins.then_inc(s_tp[l], 1)

            def graph_mlp(l, hidden, router):
                mh = hidden // P
                pe.sem_inc(s_tev[l], 2)
                pe.sem_inc(s_e1[l], 4)
                pe.sem_inc(s_e2[l], 2)
                with pe.Fori(0, NG) as g:
                    pe.wait_ge(s_ts[l], g + 1)
                    for t in range(GT):
                        turn(l, ts5, t, g * (2 * GT) + t, True)
                    pe.wait_ge(s_tev[l], g * (2 * GT) + (GT + 2))
                    pe.wait_ge(s_elg[l], g + 1)
                    for q in range(2 * mh):
                        m, (o, w) = q // 2, PIECES[q % 2]
                        pe.wait_ge(s_e1[l], g * (2 * mh) + (q + 1))
                        for k in range(KD):
                            ins = t_.matmul(PS[2 + q % 4][:, 0:w], gw1[:, k, m * P:(m + 1) * P], hT[:, k, o:o + w],
                                            start=k == 0, stop=k == KD - 1)
                        ins.then_inc(s_p1[l], 1)
                    pe.wait_ge(s_e1[l], g * (2 * mh) + (2 * mh + 4))
                    for t in range(GT):
                        pe.wait_ge(s_e2[l], g * GT + (t + 1))
                        for k in range(mh):
                            ins = t_.matmul(PS[6 + t % 2][0:TP, 0:D], gh[:, k, t * TP:(t + 1) * TP], gw2[:, k, :],
                                            start=k == 0, stop=k == mh - 1)
                        ins.then_inc(s_p2[l], 1)
                    pe.wait_ge(s_xn5[l], g + 1)
                    for t in range(GT):
                        turn(l, xn5, t, g * (2 * GT) + (GT + t), False)
                    pe.wait_ge(s_tev[l], g * (2 * GT) + (2 * GT + 2))
                    for t in range(GT):
                        for k in range(KD):
                            ins = t_.matmul(PS[2][0:TP, t * NE:(t + 1) * NE], xT5[:, k, t * TP:(t + 1) * TP], router[:, k, :],
                                            start=k == 0, stop=k == KD - 1)
                    ins.then_inc(s_plg[l], 1)

            sum_edges("l0")
            pe.wait_ge(s_w, 16 * 6)
            graph_mlp("l0", H0, gate_w)

            pe.wait_ge(s_oh, 1)
            ohf = oh[:].rearrange("p t e -> p (t e)")
            t_.matmul(PS[0][0:TP, 0:NT * NE], tri[0:TP, 0:TP], ohf, start=True, stop=True)
            t_.matmul(PS[1][0:TP, 0:NT * NE], ones[0:TP, 0:TP], ohf, start=True, stop=True).then_inc(s_ppos, 1)
            pe.wait_ge(s_route, 1)

            pe.sem_inc(s_fte, 2)
            pe.sem_inc(s_fe1, 4)
            pe.sem_inc(s_fe2, 2)
            with pe.Fori(0, NE // 2) as i:
                for b in range(2):
                    e = i * 2 + b
                    pe.wait_ge(s_fx[b], i * 32 + 32)
                    for j in range(4):
                        pe.wait_ge(s_fte, e * 4 + (j + 1))
                        for k in range(KD):
                            ins = t_.transpose(PS[j % 2][:, k * P:(k + 1) * P], xe[b][:, j, k * P:(k + 1) * P], ident[:])
                        ins.then_inc(s_ftp, 1)
                    pe.wait_ge(s_fte, e * 4 + 6)
                    pe.wait_ge(s_fw[b], i * 32 + 32)
                    for m in range(F0 // P):
                        pe.wait_ge(s_fe1, e * 8 + (m + 1))
                        for k in range(KD):
                            ins = t_.matmul(PS[2 + m % 4][:, 0:CAP], fw1[b][:, k, m * P:(m + 1) * P], xet[:, k, 0:CAP],
                                            start=k == 0, stop=k == KD - 1)
                        ins.then_inc(s_fp1, 1)
                    for j in range(4):
                        n = min(P, CAP - j * P)
                        pe.wait_ge(s_fe2, e * 4 + (j + 1))
                        for k in range(F0 // P):
                            if j == 0:
                                pe.wait_ge(s_fe1, e * 8 + (k + 5))
                            ins = t_.matmul(PS[6 + j % 2][0:n, 0:D], hid[b][:, k, j * P:j * P + n], fw2[b][:, k, :],
                                            start=k == 0, stop=k == F0 // P - 1)
                        ins.then_inc(s_fp2, 1)
                    pe.sem_inc(s_fdone, 1)

            sum_edges("l1")
            pe.wait_ge(s_w1, 32)
            graph_mlp("l1", H1, wr)

            pe.wait_ge(s_ew, 16 * 3 * NE)
            pe.wait_ge(s_ex0, 2)
            pe.sem_inc(s_ea, 4)
            pe.sem_inc(s_ec, 4)
            with pe.Fori(0, NG) as g:
                for e in range(NE):
                    for layer in range(2):
                        if layer == 1:
                            pe.wait_ge(s_ea, g * (8 * NE) + (8 * e + 8))
                        for q in range(4):
                            m, (o, w) = q // 2, PIECES[q % 2]
                            n = g * (8 * NE) + (8 * e + 4 * layer + q + 1)
                            pe.wait_ge(s_ea, n)
                            for k in range(KD):
                                rhs = XNT[:, k, ds(g * GN + o, w)] if layer == 0 else eh[e % 2][:, k, o:o + w]
                                ins = t_.matmul(PS[q][:, 0:w], WE[:, layer, e, k, m * P:(m + 1) * P], rhs,
                                                start=k == 0, stop=k == KD - 1)
                            ins.then_inc(s_pa, 1)
                    pe.wait_ge(s_ea, g * (8 * NE) + (8 * e + 12))
                    for t in range(GT):
                        r = e * GT + t
                        pe.wait_ge(s_ec, g * (NE * GT) + (r + 1))
                        for k in range(KD):
                            ins = t_.matmul(PS[4 + r % 4][0:TP, 0:D], h2buf[e % 2][:, k, t * TP:(t + 1) * TP],
                                            WE[:, 2, e, k, :], start=k == 0, stop=k == KD - 1)
                        ins.then_inc(s_pc, 1)

        @block.vector
        def _(dve):
            ch = Chain(dve, s_dve)
            v = nc.vector
            ch.link(v.memset(zeros, 0.0))
            dve.sem_inc(s_zero, 1)
            ch.link(v.memset(zero_nt[:], 0.0))

            def round_(t):
                ch.link(v.tensor_scalar(t, t, MAGIC, None, ALU.add))
                ch.link(v.tensor_scalar(t, t, MAGIC, None, ALU.subtract))

            dve.wait_ge(s_e, 48)
            ch.link(v.tensor_copy(srcf, esrc))
            ch.link(v.tensor_scalar(tile_of, srcf, -float(TP // 2), 1.0 / TP, ALU.add, ALU.mult))
            round_(tile_of)
            ch.link(v.scalar_tensor_tensor(out=recs[:, :, 0], in0=tile_of, scalar=-float(TP), in1=srcf,
                                           op0=ALU.mult, op1=ALU.add))
            v.tensor_copy(recs[:, :, 1], edst)
            v.tensor_copy(recs[:, :, 2], ew)
            v.memset(recs[:, :, 3], 0.0)
            ch.link(v.memset(loc, -1.0))
            for b in range(NT):
                ch.link(v.tensor_scalar(mask, tile_of, float(b), None, ALU.is_equal))
                ch.link(v.tensor_tensor_scan(rank, mask, mask, 0.0, ALU.add, ALU.bypass))
                v.tensor_copy(cnt[:, b:b + 1], rank[:, EC - 1:EC])
                ch.link(v.tensor_tensor(mask, rank, mask, ALU.mult))
                ch.link(v.tensor_tensor(loc, loc, mask, ALU.add))
            dve.sem_inc(s_cnt, 1)
            dve.wait_ge(s_pre, 1)
            ch.link(v.tensor_scalar(nch[:], PS[1][0:EP, 0:NT], CH - 1 - (CH - 1) / 2, 1.0 / CH, ALU.add, ALU.mult))
            round_(nch[:])
            ch.link(v.tensor_tensor_scan(cend[:], nch[:], zero_nt[:], 0.0, ALU.add, ALU.add))
            ch.link(v.tensor_tensor(cbase[:], cend[:], nch[:], ALU.subtract))
            ch.link(v.scalar_tensor_tensor(out=cbase[:], in0=cbase[:], scalar=float(CH), in1=PS[0][0:EP, 0:NT],
                                           op0=ALU.mult, op1=ALU.add))
            for b in range(NT):
                ch.link(v.tensor_scalar(mask, tile_of, float(b), cbase[:, b:b + 1], ALU.is_equal, ALU.mult))
                ch.link(v.tensor_tensor(loc, loc, mask, ALU.add))
            ch.link(v.tensor_scalar(mask, loc, -(CH - 1) / 2, 1.0 / CH, ALU.add, ALU.mult))
            round_(mask)
            ch.link(v.scalar_tensor_tensor(out=loc, in0=mask, scalar=-float(CH), in1=loc, op0=ALU.mult, op1=ALU.add))
            ch.link(v.scalar_tensor_tensor(out=pos, in0=loc, scalar=float(NCH), in1=mask, op0=ALU.mult, op1=ALU.add))
            dve.sem_inc(s_pos, 1)
            ch.link(v.memset(chunk_tile[:], 0.0))
            dve.wait_ge(s_const, 1)
            for b in range(NT - 1):
                ch.link(v.scalar_tensor_tensor(out=chunk_tile[:], in0=ciota[:], scalar=cend[0:1, b:b + 1],
                                               in1=chunk_tile[:], op0=ALU.is_ge, op1=ALU.add))
            ch.link(v.tensor_copy(chunk_tile_i[:], chunk_tile[:]))
            ch.link(v.memset(trec[:, NCH:, :], 0.0))

            dve.wait_ge(s_w, 16 * 6)
            for l in (1, 2):
                ch.link(v.tensor_scalar(bn[:, 2 * l - 2, :], col(f"v{l}"), 1e-3, None, ALU.add))
            dve.sem_inc(s_bn, 1)
            dve.wait_ge(s_bn, 2)
            for l in (1, 2):
                ch.link(v.reciprocal(bnt[:], bn[:, 2 * l - 2, :]))
                ch.link(v.tensor_tensor(bn[:, 2 * l - 2, :], bnt[:], col(f"g{l}"), ALU.mult))
                ch.link(v.tensor_tensor(bnt[:], col(f"b{l}"), col(f"m{l}"), ALU.subtract))
                ch.link(v.tensor_tensor(bnt[:], bnt[:], bn[:, 2 * l - 2, :], ALU.mult))
                ch.link(v.tensor_tensor(bn[:, 2 * l - 1, :], bnt[:], col(f"be{l}"), ALU.add))

            NORM = 5

            def norm(src, dst, n, eps):
                dve.sem_inc(s_step["dve"], 1)
                for t in range(GT):
                    ins = v.bn_stats(st5[:, t, :], src(t))
                ch.link(ins)
                dve.sem_inc(s_step["dve"], 1)
                for t in range(GT):
                    ins = v.bn_aggr(mv5[:, t, :], st5[:, t, :])
                ch.link(ins)
                ch.link(v.tensor_scalar(var5[:], mv5[:, :, 1], eps, None, ALU.add))
                dve.sem_inc(s_var, 1)
                dve.wait_ge(s_std, n)
                ch.link(v.reciprocal(rstd5[:], std5[:]))
                for t in range(GT):
                    ins = v.tensor_scalar(dst(t), src(t), mv5[:, t, 0:1], rstd5[:, t:t + 1], ALU.subtract, ALU.mult)
                ch.link(ins)

            def x_tile(base, t):
                return base[:, ds(t, 1), :].rearrange("p a d -> p (a d)")

            dve.wait_ge(s_x, 16)
            with dve.Fori(0, NG) as g:
                ch.enter(g, NORM)
                norm(lambda t: x_tile(X, g * GT + t), lambda t: x_tile(AGG, g * GT + t), g + 1, 1e-5)
            ch.leave(NG)
            dve.sem_inc(s_xn["l0"], 1)
            ch.link(v.tensor_tensor(X[:], X[:], bcast(row("g0b2"), NT, D), ALU.add))

            def sum_edges(l):
                dve.wait_ge(s_rec, 16)
                dve.wait_ge(s_xns[l], 16)

                def make_pick(c, u):
                    v.tensor_scalar(pick[:, u, :], iota_row[:], trec[:, ds(c, 1), 0:1].rearrange("p a w -> p (a w)"),
                                    trec[:, ds(c, 1), 2:3].rearrange("p a w -> p (a w)"),
                                    ALU.is_equal, ALU.mult).then_inc(s_pick[l], 1)

                def add_chunk(c, u):
                    dve.wait_ge(s_mm[l], c + 1)
                    dve.wait_ge(s_acc[l], c + BANKS)
                    t = dve.value_load(chunk_tile_i[0:1, ds(c, 1)], min_val=0, max_val=NT - 1)
                    v.tensor_tensor(x_tile(AGG, t), x_tile(AGG, t), PS[u % BANKS][0:TP, 0:D], ALU.add).then_inc(s_acc[l], 1)

                dve.sem_inc(s_acc[l], BANKS)
                H = STAGE
                for u in range(H):
                    make_pick(u, u)
                with dve.Fori(0, NCH // RING) as i:
                    for u in range(H):
                        make_pick(i * RING + (H + u), H + u)
                        add_chunk(i * RING + u, u)
                    for u in range(H):
                        make_pick(i * RING + (RING + u), u)
                        add_chunk(i * RING + (H + u), H + u)
                dve.wait_ge(s_acc[l], NCH + BANKS)

            sum_edges("l0")

            def graph_mlp(l, per, norms):
                dve.sem_inc(s_elg[l], 1)
                with dve.Fori(0, NG) as g:
                    ch.enter(g, per)
                    ch.link(v.tensor_copy(ts5, AGG[:, ds(g * GT, GT), :]))
                    dve.sem_inc(s_ts[l], 1)
                    if l == "l0":
                        for t in range(GT):
                            dve.wait_ge(s_p2[l], g * GT + (t + 1))
                            ins = v.tensor_tensor(x_tile(X, g * GT + t), x_tile(X, g * GT + t), PS[6 + t % 2][0:TP, 0:D], ALU.add)
                            ins.then_inc(s_e2[l], 1)
                        dve.wait_ge(s_e2[l], g * GT + (GT + 2))
                        norm(lambda t: x_tile(X, g * GT + t), lambda t: xn5[:, t, :], g + (norms + 1), 1e-5)
                    else:
                        b5 = big.rearrange("p (t d) -> p t d", t=GT)
                        for t in range(GT):
                            dve.wait_ge(s_p2[l], g * GT + (t + 1))
                            v.tensor_tensor(b5[:, t, :], PS[6 + t % 2][0:TP, 0:D], row("g1b2"), ALU.add).then_inc(s_e2[l], 1)
                        dve.wait_ge(s_e2[l], g * GT + (GT + 2))
                        ch.link(v.tensor_scalar(big, big, 0.0, None, ALU.max))
                        norm(lambda t: b5[:, t, :], lambda t: b5[:, t, :], g * 2 + (norms + 1), 1e-10)
                        ch.link(v.tensor_tensor(b5, b5, bcast(row("scale"), GT, D), ALU.mult))
                        ch.link(v.tensor_tensor(X[:, ds(g * GT, GT), :], X[:, ds(g * GT, GT), :], b5, ALU.add))
                        norm(lambda t: x_tile(X, g * GT + t), lambda t: xn5[:, t, :], g * 2 + (norms + 2), 1e-5)
                    dve.sem_inc(s_xn5[l], 1)
                    if l == "l0":
                        ch.link(v.tensor_copy(AGG[:, ds(g * GT, GT), :], xn5))
                    dve.wait_ge(s_plg[l], g + 1)
                    if l == "l1":
                        v.tensor_copy(XNT[:, :, ds(g * GN, GN)], xT5)
                    ch.link(v.tensor_copy(LG[:, ds(g * GT, GT), :],
                                          PS[2][0:TP, 0:GT * NE].rearrange("p (t e) -> p t e", t=GT)))
                    dve.sem_inc(s_elg[l], 1)
                ch.leave(NG)

            graph_mlp("l0", 1 + NORM + 2, NG)

            def softmax_in(bias):
                ch.link(v.tensor_tensor(LG[:], LG[:], bcast(bias, NT, NE), ALU.add))
                ch.link(v.tensor_reduce(mx[:], LG[:], AX.X, ALU.max))
                ch.link(v.tensor_tensor(ex[:], LG[:], bcast_in(mx[:], NE), ALU.subtract))
                dve.sem_inc(s_ex0, 1)

            softmax_in(row("gate_b"))
            ch.link(v.tensor_tensor(oh[:], LG[:], bcast_in(mx[:], NE), ALU.is_equal))
            ch.link(v.tensor_tensor(oh[:], oh[:], bcast(rev[:], NT, NE), ALU.mult))
            ch.link(v.tensor_reduce(rt[:, 0, :], oh[:], AX.X, ALU.max))
            ch.link(v.tensor_tensor(oh[:], bcast(rev[:], NT, NE), bcast_in(rt[:, 0, :], NE), ALU.is_equal))
            dve.sem_inc(s_oh, 1)
            dve.wait_ge(s_ppos, 1)
            pt = PS[1][0:TP, 0:NT * NE].rearrange("p (t e) -> p t e", t=NT)
            pp = PS[0][0:TP, 0:NT * NE].rearrange("p (t e) -> p t e", t=NT)
            ch.link(v.tensor_copy(px[:], pt))
            for e in range(NE):
                ins = v.tensor_tensor_scan(ctot[:, :, e], px[:, :, e], zero_nt[:], 0.0, ALU.add, ALU.add)
            ch.link(ins)
            ch.link(v.tensor_tensor(ctot[:], ctot[:], px[:], ALU.subtract))
            ch.link(v.tensor_tensor(ctot[:], ctot[:], pp, ALU.add))
            ch.link(v.tensor_tensor(ctot[:], ctot[:], oh[:], ALU.mult))
            ch.link(v.tensor_reduce(rt[:, 1, :], ctot[:], AX.X, ALU.add))
            ch.link(v.tensor_scalar(rt[:, 2, :], rt[:, 1, :], float(CAP), None, ALU.is_lt))
            ch.link(v.tensor_scalar(rt[:, 3, :], rt[:, 0, :], -float(SLOTS), float(TRASH), ALU.mult, ALU.add))
            ch.link(v.tensor_scalar(rt[:, 4, :], rt[:, 0, :], -float(CAP), float(NE * CAP), ALU.mult, ALU.add))
            ch.link(v.scalar_tensor_tensor(out=rti[:, 1, :], in0=rt[:, 1, :], scalar=float(CAP - 1), in1=rt[:, 4, :],
                                           op0=ALU.min, op1=ALU.add))
            ch.link(v.tensor_tensor(rt[:, 4, :], rt[:, 1, :], rt[:, 3, :], ALU.add))
            ch.link(v.tensor_tensor(rt[:, 4, :], rt[:, 4, :], trash[:], ALU.subtract))
            ch.link(v.tensor_tensor(rt[:, 4, :], rt[:, 4, :], rt[:, 2, :], ALU.mult))
            ch.link(v.tensor_tensor(rti[:, 0, :], rt[:, 4, :], trash[:], ALU.add))
            dve.wait_ge(s_ex1, 1)
            ch.link(v.tensor_reduce(rt[:, 5, :], ex[:], AX.X, ALU.add))
            ch.link(v.reciprocal(rt[:, 6, :], rt[:, 5, :]))
            ch.link(v.tensor_tensor(rt[:, 7, :], rt[:, 6, :], rt[:, 2, :], ALU.mult))
            dve.sem_inc(s_route, 1)

            def expert_out(i, first):
                for b in range(2):
                    e = i * 2 + b
                    dve.wait_ge(s_fx[b], i * 32 + 32)
                    if not first:
                        dve.wait_ge(s_ys[b], i * 32)
                    for j in range(4):
                        n = min(P, CAP - j * P)
                        dve.wait_ge(s_fp2, e * 4 + (j + 1))
                        v.tensor_tensor(yo[b][0:n, j, :], PS[6 + j % 2][0:n, 0:D], fb2[b][0:n, :], ALU.add).then_inc(s_fe2, 1)

            expert_out(0, True)
            with dve.Fori(1, NE // 2) as i:
                expert_out(i, False)

            dve.wait_ge(s_tok, 16 * NT)
            for g in range(NG):
                dve.wait_ge(s_yg[g], 16 * GT)
                yg = YG[:, g * GT:(g + 1) * GT, :]
                yf = yg.rearrange("p t d -> p (t d)")
                for t in range(GT):
                    n = g * GT + t
                    ins = v.tensor_scalar(YG[:, n, :], YG[:, n, :], rt[:, 7, n:n + 1], None, ALU.mult)
                ch.link(ins)
                v.tensor_scalar(fin, yf, 0.0, 0.0, ALU.mult, ALU.is_equal)
                ch.link(v.tensor_tensor(big, yf, yf, ALU.is_equal))
                ch.link(v.tensor_scalar(clamped, yf, -10000.0, 10000.0, ALU.max, ALU.min))
                ch.link(v.tensor_tensor(clamped, clamped, big, ALU.mult))
                ch.link(v.copy_predicated(clamped, fin, yf))
                xg = X[:, g * GT:(g + 1) * GT, :]
                ch.link(v.tensor_tensor(xg, xg, clamped.rearrange("p (t d) -> p t d", t=GT), ALU.add))
                dve.sem_inc(s_ygused, 1)
            with dve.Fori(0, NG) as g:
                ch.enter(g, NORM)
                norm(lambda t: x_tile(X, g * GT + t), lambda t: x_tile(AGG, g * GT + t), g + (2 * NG + 1), 1e-5)
            ch.leave(NG)
            dve.sem_inc(s_xn["l1"], 1)
            ch.link(v.tensor_tensor(X[:], X[:], bcast(row("offset"), NT, D), ALU.add))
            ch.link(v.tensor_scalar(rt[:, 0, 0:1], row("eps"), 1.0, None, ALU.add))
            dve.wait_ge(s_xns["l1"], 16)
            ch.link(v.tensor_scalar(AGG[:], AGG[:], rt[:, 0, 0:1], None, ALU.mult))
            sum_edges("l1")
            graph_mlp("l1", 1 + 1 + NORM + 2 + NORM + 1, 3 * NG)

            softmax_in(row("br"))
            dve.wait_ge(s_ex1, 2)
            ch.link(v.tensor_reduce(rt[:, 5, :], ex[:], AX.X, ALU.add))
            ch.link(v.reciprocal(rt[:, 6, :], rt[:, 5, :]))
            ch.link(v.tensor_tensor(GW[:], ex[:], bcast_in(rt[:, 6, :], NE), ALU.mult))
            dve.wait_ge(s_bo, 16)
            with dve.Fori(0, NG) as g:
                for e in range(NE):
                    for t in range(GT):
                        r = e * GT + t
                        xt = x_tile(X, g * GT + t)
                        gw = GW[:, ds(g * GT + t, 1), e:e + 1].rearrange("p a b -> p (a b)")
                        dve.wait_ge(s_pc, g * (NE * GT) + (r + 1))
                        v.scalar_tensor_tensor(out=xt, in0=PS[4 + r % 4][0:TP, 0:D], scalar=gw, in1=xt,
                                               op0=ALU.mult, op1=ALU.add).then_inc(s_ec, 1)
                    dve.wait_ge(s_ec, g * (NE * GT) + (e * GT + GT + 4))
                    for t in range(GT):
                        xt = x_tile(X, g * GT + t)
                        gw = GW[:, ds(g * GT + t, 1), e:e + 1].rearrange("p a b -> p (a b)")
                        ins = v.scalar_tensor_tensor(out=xt, in0=bo_b[:, e, :], scalar=gw, in1=xt,
                                                     op0=ALU.mult, op1=ALU.add)
                    ins.then_inc(s_dve, 1)
                    dve.wait_ge(s_dve, g * NE + (ch.n + e + 1))
                dve.sem_inc(s_res, 1)


_INS = ["x", "src", "dst", "edge_weight", "L0_gnn_W1", "L0_gnn_W2", "L0_ffn_gate_w", "L0_ffn_w1", "L0_ffn_w2", "L0_ffn_b2",
        "L1_gnn_W1", "L1_gnn_W2", "L1_ffn_Wr", "L1_ffn_W1", "L1_ffn_W2", "L1_ffn_Wo", "L1_ffn_bo"]


def kernel(**inputs):
    import numpy as _np
    import concourse.bacc as _bacc
    from concourse import mybir as _mybir
    from concourse.bass_utils import run_bass_kernel_spmd as _run

    arrays = {name: _np.ascontiguousarray(inputs[name]) for name in _INS}

    def columns(v):
        return _np.asarray(v).reshape(-1, P).T

    arrays["cols"] = _np.ascontiguousarray(_np.concatenate([
        columns(inputs["L0_gnn_b1"]), columns(inputs["L0_ffn_b1"]), columns(inputs["L1_gnn_b1"]),
        *(columns(inputs[f"L1_ffn_{v}{l}"]) for l in (1, 2) for v in ("g", "be", "m", "v", "b"))], axis=1))
    arrays["rows"] = _np.concatenate([_np.asarray(inputs[n]) for n in (
        "L0_gnn_b2", "L1_gnn_b2", "L1_gnn_offset", "L1_gnn_scale", "L0_ffn_gate_b", "L1_ffn_br", "L1_gnn_eps")])
    nc = _bacc.Bacc("TRN2", target_bir_lowering=False, num_devices=1)
    args = {n: nc.dram_tensor(f"in_{n}_dram", v.shape, _mybir.dt.from_np(v.dtype), kind="ExternalInput").ap()
            for n, v in arrays.items()}
    out = nc.dram_tensor("out_0_dram", (N, D), _mybir.dt.float32, kind="ExternalOutput").ap()
    program(nc, args, out)
    r = _run(nc, [{f"in_{n}_dram": v for n, v in arrays.items()}], core_ids=[0])
    return r.results[0]["out_0_dram"]
```
